# Optimizing a Trainium2 kernel written in Bass

```python
import numpy as np
import jax
import jax.numpy as jnp

def _softmax(x, axis=-1):
    return jax.nn.softmax(x, axis=axis)
def _gelu(x):
    return jax.nn.gelu(x, approximate=True)
def _silu(x):
    return jax.nn.silu(x)
def _sigmoid(x):
    return jax.nn.sigmoid(x)
def _layernorm(x, axis=-1, eps=1e-5):
    m = jnp.mean(x, axis=axis, keepdims=True)
    v = jnp.var(x, axis=axis, keepdims=True)
    return (x - m) / jnp.sqrt(v + eps)
def _scatter_add(tgt, idx, src, axis=0):
    return tgt.at[idx].add(src)
def _segment_sum(src, seg, n):
    return jax.ops.segment_sum(src, seg, n)

kernel_name = 'mk_adj_preln_d2_adj_128_7e5ce6'

def setup_inputs(seed: int = 0):
    np.random.seed(seed)
    _w = jnp.asarray
    def _rec_inputs():
        import jax
        import jax.numpy as jnp
        _gk = jax.random.key(seed)
        x = -0.000929 + 1 * jax.random.normal(jax.random.fold_in(_gk, 1), (3327, 128), jnp.float32)
        _w = (1.0 + jnp.arange(3327, dtype=jnp.float32)) ** -0.5
        _w = _w / _w.mean()
        _pij = jnp.clip(0.00120228 * _w[:, None] * _w[None, :], 0.0, 1.0)
        _a = jax.random.uniform(jax.random.fold_in(_gk, 2), (3327, 3327)) < _pij
        _a = jnp.logical_or(_a, jnp.eye(3327, dtype=bool))
        _af = _a.astype(jnp.float32)
        _af = _af * jax.random.uniform(jax.random.fold_in(_gk, 3), (3327, 3327), jnp.float32, 0.05, 1)
        adj = _af
        return x, adj
    x, adj = _rec_inputs()
    def _L0_gnn_setup():
        import jax, jax.numpy as jnp
        import numpy as np
        N = 8192
        F = 128
        key = jax.random.key(seed)
        k1, k2, k3 = jax.random.split(key, 3)
        x = jax.random.normal(k1, (N, F), dtype=jnp.float32)
        adj = jax.random.uniform(k2, (N, N), dtype=jnp.float32)
        limit = float(np.sqrt(6.0 / (F + F)))
        weight = jax.random.uniform(k3, (F, F), dtype=jnp.float32, minval=-limit, maxval=limit)
        return {'x': x, 'adj': adj, 'weight': weight}
    _L0_gnn_all = _L0_gnn_setup()
    _L0_gnn_in = {k: v for k, v in _L0_gnn_all.items() if k in ('weight', )}
    del _L0_gnn_all

    def _L1_gnn_setup():
        import jax, jax.numpy as jnp
        import numpy as np
        N = 1024
        D = 128
        H = 8
        key = jax.random.key(seed)
        ks = jax.random.split(key, 7)
        s = (D * H) ** (-0.5)
        return {'x': jax.random.normal(ks[0], (N, D), dtype=jnp.float32), 'spatial_encoding': jax.random.normal(ks[1], (N, N), dtype=jnp.float32), 'edge_encoding': jax.random.normal(ks[2], (N, N), dtype=jnp.float32), 'Wq': jax.random.normal(ks[3], (D * H, D), dtype=jnp.float32) * s, 'Wk': jax.random.normal(ks[4], (D * H, D), dtype=jnp.float32) * s, 'Wv': jax.random.normal(ks[5], (D * H, D), dtype=jnp.float32) * s, 'Wo': jax.random.normal(ks[6], (D, D * H), dtype=jnp.float32) * s}
    _L1_gnn_all = _L1_gnn_setup()
    _L1_gnn_in = {k: v for k, v in _L1_gnn_all.items() if k in ('Wq', 'Wk', 'Wv', 'Wo', )}
    del _L1_gnn_all

    return {
        "x": x,
        "adj": adj,
        "L0_gnn_weight": _L0_gnn_in["weight"],
        "L1_gnn_Wq": _L1_gnn_in["Wq"],
        "L1_gnn_Wk": _L1_gnn_in["Wk"],
        "L1_gnn_Wv": _L1_gnn_in["Wv"],
        "L1_gnn_Wo": _L1_gnn_in["Wo"],
    }

def reference(x, adj, L0_gnn_weight, L1_gnn_Wq, L1_gnn_Wk, L1_gnn_Wv, L1_gnn_Wo):
    import jax
    import jax.numpy as jnp
    def _L0_gnn_ref(x, adj, weight):
        import jax, jax.numpy as jnp
        import numpy as np
        N = 8192
        F = 128
        n = adj.shape[0]
        adj_hat = adj + jnp.eye(n, dtype=adj.dtype)
        deg = jnp.sum(adj_hat, axis=1)
        d_inv_sqrt = (deg + 1e-08) ** (-0.5)
        support = d_inv_sqrt[:, None] * adj_hat * d_inv_sqrt[None, :]
        out = jnp.matmul(jnp.matmul(support, x), weight)
        return jax.nn.relu(out)

    def _L1_gnn_ref(x, spatial_encoding, edge_encoding, Wq, Wk, Wv, Wo):
        import jax, jax.numpy as jnp
        import numpy as np
        N = 1024
        D = 128
        H = 8
        n, d = x.shape
        h = Wq.shape[0] // d
        scale = d ** (-0.5)
        q = (x @ Wq.T).reshape(d, n, h)
        k = (x @ Wk.T).reshape(d, n, h)
        v = (x @ Wv.T).reshape(d, n, h)
        a = jnp.einsum('dnh,dmh->dnm', q, k) * scale
        a = a + spatial_encoding + edge_encoding
        a = jax.nn.softmax(a, axis=2)
        out = jnp.einsum('dnm,dmh->dnh', a, v)
        out = out.reshape(n, h * d)
        return out @ Wo.T

    h = jnp.maximum(_layernorm(x, axis=-1), 0.0)
    x = x + _L0_gnn_ref(h, adj, L0_gnn_weight)
    h = jnp.maximum(_layernorm(x, axis=-1), 0.0)
    x = x + _L1_gnn_ref(h, adj, adj, L1_gnn_Wq, L1_gnn_Wk, L1_gnn_Wv, L1_gnn_Wo)
    return x


_drawn_inputs = setup_inputs


def setup_inputs(seed=0):
    import zlib

    import numpy as np

    out = dict(_drawn_inputs(seed))
    spreads = {}
    factors = {'L1_gnn_Wq': 8.0, 'L1_gnn_Wk': 8.0, 'L1_gnn_Wv': 6.345, 'L1_gnn_Wo': 8.0}
    for name, (base, spread) in spreads.items():
        noise = np.random.default_rng([zlib.crc32(name.encode()), seed]).standard_normal(out[name].shape)
        drawn = base * np.exp(spread * noise) if base else spread * noise
        out[name] = jnp.asarray(drawn.astype(out[name].dtype))
    for name, factor in factors.items():
        out[name] = (out[name] * factor).astype(out[name].dtype)
    return out
```

```python
import concourse.bass as bass
from concourse import mybir
from contextlib import ExitStack


def graph_layers_kernel(nc, x, adj, w0, wq, wk, wv, wo, out):
    fp32 = mybir.dt.float32
    bf16 = mybir.dt.bfloat16
    ACT = mybir.ActivationFunctionType
    ALU = mybir.AluOpType
    AX = mybir.AxisListType

    N, F = x.shape
    P = 128
    NT = (N + P - 1) // P
    NP = NT * P
    LAST = N - (NT - 1) * P
    H = wq.shape[0] // F
    HEADS = F
    GH = 16
    NG = HEADS // GH
    NB = 8
    CB = NP // NB
    CS = CB // 4
    NPAIR = NT // 2
    NCH = 4
    CH = NP // NCH
    BODIES = NT
    KR = 6 * H
    XR = 88
    SLOTS = 8
    GP = NP * P
    HALF_SCALE = float(F) ** -0.5 / 2
    FAR = -1.0e30
    LOW = -3.0e38
    EPS = 1e-5

    def dram(name, shape, dt):
        return nc.dram_tensor(name, shape, dt)

    adjp_t = dram("adj_padded", (NP, NP), fp32)
    q_t = dram("q_planes", (6 * H, GP), bf16)
    k_t = dram("k_planes", (3 * H, GP), bf16)
    v_t = dram("v_planes", (H, GP), fp32)
    vt_t = dram("v_by_key", (NG * NP, GH * H), fp32)
    m_t = dram("maxima", (6, HEADS, NP), bf16)
    o_t = dram("head_out", (NG * 2 * P, NP), fp32)
    oh_t = dram("out_planes", (H, GP), fp32)
    adjp, vt, mx, ost = adjp_t.ap(), vt_t.ap(), m_t.ap(), o_t.ap()

    def by_head(t, rows):
        return bass.AP(t, 0, [[GP, rows], [N, HEADS], [1, NP]])

    q_heads, k_heads, v_heads = by_head(q_t, 6 * H), by_head(k_t, 3 * H), by_head(v_t, H)

    def by_row(t, rows):
        return t.ap().rearrange("r (i b) -> i r b", b=P)

    q_rows, k_rows, v_rows, oh_rows = (by_row(t, r) for t, r in ((q_t, 48), (k_t, 24), (v_t, H), (oh_t, H)))

    ds = bass.ds

    def identity(pool, tile, n, ready, done):
        pool.memset(tile, 0.0).then_inc(ready, 1)
        wait(pool, ready, 1)
        pool.affine_select(out=tile, in_=tile, compare_op=ALU.not_equal, fill=1.0, base=0,
                           pattern=[[-1, n]], channel_multiplier=1).then_inc(done, 1)

    top = ExitStack()
    gate = {}

    def wait(eng, sem, value):
        eng.wait_ge(sem, value)
        if not isinstance(value, int):
            eng.sem_inc(gate[0], 1)

    with top:
        gate[0] = top.enter_context(nc.semaphore("s_gate"))

        def open_(ctx):
            return (lambda n, s, d: ctx.enter_context(nc.sbuf_tensor(n, s, d)),
                    lambda n, s, d: ctx.enter_context(nc.psum_tensor(n, s, d)),
                    lambda n: ctx.enter_context(nc.semaphore(n)))

        with ExitStack() as outer:
            sb, pb, sem = open_(outer)
            xs = sb("xs", [P, NT, F], fp32)
            hn = sb("hn", [P, NT, F], fp32)
            o2 = sb("o2", [P, NT, F], fp32)
            ident = sb("ident", [P, P], fp32)
            x1_t = dram("x_after_0", (NP, F), fp32)
            x1_rows = x1_t.ap().rearrange("(t p) f -> p t f", p=P)

            def layer_norm(dve, link, src, stats, mv, rstd_ready_wait, var_inc, rstd):
                for t in range(NT):
                    last = nc.vector.bn_stats(stats[:, t, :], src[:, t, :])
                link(last)
                for t in range(NT):
                    last = nc.vector.bn_aggr(mv[:, t, :], stats[:, t, :])
                link(last)
                link(nc.vector.tensor_tensor(hn[:], src[:], mv[:, :, 0:1].to_broadcast((P, NT, F)), ALU.subtract))
                nc.vector.tensor_scalar(rstd[:], mv[:, :, 1], EPS, None, ALU.add).then_inc(var_inc, 1)
                rstd_ready_wait()
                link(nc.vector.tensor_tensor(hn[:], hn[:], rstd[:].unsqueeze(2).to_broadcast((P, NT, F)), ALU.mult))

            with ExitStack() as c1:
                sb, pb, sem = open_(c1)
                row = [sb(f"row{i}", [P, NP], fp32) for i in range(2)]
                aT = sb("aT", [P, NT, P], fp32)
                w0s = sb("w0s", [F, F], fp32)
                aggs = sb("aggs", [F, P], fp32)
                deg = sb("deg", [P, NT], fp32)
                dis = sb("dis", [P, NT], fp32)
                expo = sb("expo", [P, NT], fp32)
                stats = sb("stats", [P, NT, 6], fp32)
                mv = sb("mv", [P, NT, 2], fp32)
                rstd = sb("rstd", [P, NT], fp32)
                tr = [pb(f"tr{i}", [P, 512], fp32) for i in range(2)]
                agg = pb("agg", [P, 512], fp32)
                upd = pb("upd", [P, 512], fp32)
                s_zero = sem("s_zero")
                s_id = sem("s_id")
                s_pad = sem("s_pad")
                s_xp = sem("s_xp")
                s_x = sem("s_x")
                s_ld = [sem(f"s_ld{i}") for i in range(2)]
                s_ll = sem("s_ll")
                s_st = [sem(f"s_st{i}") for i in range(2)]
                s_deg = sem("s_deg")
                s_lnv = sem("s_lnv")
                s_rstd = sem("s_rstd")
                s_d = sem("s_d")
                s_c = sem("s_c")
                s_h = sem("s_h")
                s_lb = [sem(f"s_lb{i}") for i in range(2)]
                s_eye = sem("s_eye")
                s_tr0, s_tr1 = sem("s_tr0"), sem("s_tr1")
                s_ev0, s_ev1 = sem("s_ev0"), sem("s_ev1")
                s_ag = sem("s_ag")
                s_agc = sem("s_agc")
                s_u = sem("s_u")
                s_uc = sem("s_uc")
                GROUPS = [(4 * i, min(4, NT - 4 * i)) for i in range((NT + 3) // 4)]
                EVEN, ODD = (len(GROUPS) + 1) // 2, len(GROUPS) // 2

                with nc.Block() as block:
                    @block.sync
                    def _(sp):
                        sp.dma_start(xs[:, 0:NT - 1, :], x[0:(NT - 1) * P, :].rearrange("(t p) f -> p t f", p=P)).then_inc(s_x, 16)
                        wait(sp, s_xp, 1)
                        sp.dma_start(xs[0:LAST, NT - 1, :], x[(NT - 1) * P:N, :]).then_inc(s_x, 16)
                        sp.dma_start(w0s[:], w0[:, :]).then_inc(s_x, 16)

                        def load(k, s, t):
                            wait(sp, s_st[s], 16 * k)
                            wait(sp, s_deg, 2 * k + s)
                            sp.dma_start(row[s][:, 0:N], adj[ds(t * P, P), :]).then_inc(s_ld[s], 16)
                        for s in range(2):
                            sp.dma_start(row[s][:, 0:N], adj[s * P:(s + 1) * P, :]).then_inc(s_ld[s], 16)
                        with sp.Fori(1, NT // 2 - 1) as k:
                            for s in range(2):
                                load(k, s, 2 * k + s)
                        k = NT // 2 - 1
                        load(k, 0, NT - 2)
                        wait(sp, s_st[1], 16 * k)
                        wait(sp, s_deg, 2 * k + 1)
                        sp.dma_start(row[1][0:112, 0:N], adj[(NT - 1) * P:(NT - 1) * P + 112, :]).then_inc(s_ll, 16)
                        sp.dma_start(row[1][112:LAST, 0:N], adj[(NT - 1) * P + 112:N, :]).then_inc(s_ll, 16)
                        for s in range(2):
                            wait(sp, s_st[s], 16 * (NT // 2))
                        wait(sp, s_deg, NT + 1)
                        for s in range(2):
                            sp.dma_start(row[s][:], adjp[s * P:(s + 1) * P, :]).then_inc(s_lb[s], 16)
                        with sp.Fori(1, NT // 2) as k:
                            for s in range(2):
                                wait(sp, s_ag, (2 * k + s - 1) * len(GROUPS) + 7)
                                sp.dma_start(row[s][:], adjp[ds((2 * k + s) * P, P), :]).then_inc(s_lb[s], 16)

                    @block.gpsimd
                    def _(pool):
                        for s in range(2):
                            pool.memset(row[s][:, N:NP], FAR).then_inc(s_pad, 1)
                        pool.memset(expo[:], -0.5).then_inc(s_pad, 1)
                        identity(pool, ident[:], P, s_zero, s_id)
                        wait(pool, s_lnv, 1)
                        wait(pool, s_pad, 3)
                        nc.gpsimd.tensor_tensor(rstd[:], rstd[:], expo[:], ALU.pow).then_inc(s_rstd, 1)
                        wait(pool, s_deg, NT + 1)
                        nc.gpsimd.tensor_tensor(dis[:], deg[:], expo[:], ALU.pow).then_inc(s_d, 1)

                    @block.scalar
                    def _(act):
                        act.sem_inc(s_ev0, 1)
                        act.sem_inc(s_agc, 1)
                        act.wait_ge(s_pad, 2)
                        with act.Fori(0, NT // 2 - 1) as k:
                            for s in range(2):
                                act.wait_ge(s_ld[s], 16 * k + 16)
                                act.dma_start(adjp[ds((2 * k + s) * P, P), :], row[s][:]).then_inc(s_st[s], 16)
                        act.wait_ge(s_ld[0], 16 * (NT // 2))
                        act.dma_start(adjp[NP - 2 * P:NP - P, :], row[0][:]).then_inc(s_st[0], 16)
                        act.wait_ge(s_ll, 32)
                        act.dma_start(adjp[NP - P:NP, :], row[1][:]).then_inc(s_st[1], 16)
                        with act.Fori(0, NT) as t:
                            for e in range(EVEN):
                                g0, n = GROUPS[2 * e]
                                act.wait_ge(s_tr0, EVEN * t + e + 1)
                                act.wait_ge(s_ag, len(GROUPS) * t + 2 * e + 1)
                                nc.scalar.activation(aT[:, g0:g0 + n, :], tr[0][:, 0:n * P].rearrange("p (a b) -> p a b", b=P), ACT.Copy).then_inc(s_ev0, 1)
                            act.wait_ge(s_ag, len(GROUPS) * (t + 1) + 7)
                            nc.scalar.activation(aggs[:], agg[:, 0:P], ACT.Copy).then_inc(s_agc, 1)

                    @block.vector
                    def _(dve):
                        chain = [0]

                        def link(ins):
                            chain[0] += 1
                            ins.then_inc(s_c, 1)
                            dve.wait_ge(s_c, chain[0])

                        dve.sem_inc(s_ev1, 1)
                        dve.sem_inc(s_uc, 1)
                        nc.vector.memset(xs[96:P, NT - 1, :], 0.0).then_inc(s_xp, 1)
                        with dve.Fori(0, NT // 2 - 1) as k:
                            for s in range(2):
                                dve.wait_ge(s_ld[s], 16 * k + 16)
                                nc.vector.reduce_sum(deg[:, ds(2 * k + s, 1)], row[s][:, 0:N], AX.X).then_inc(s_deg, 1)
                        k = NT // 2 - 1
                        dve.wait_ge(s_ld[0], 16 * (k + 1))
                        nc.vector.reduce_sum(deg[:, NT - 2:NT - 1], row[0][:, 0:N], AX.X).then_inc(s_deg, 1)
                        dve.wait_ge(s_ll, 32)
                        nc.vector.reduce_sum(deg[:, NT - 1:NT], row[1][:, 0:N], AX.X).then_inc(s_deg, 1)
                        dve.wait_ge(s_deg, NT)
                        nc.vector.tensor_scalar(deg[:], deg[:], 1.0, 1e-8, ALU.add, ALU.add).then_inc(s_deg, 1)
                        dve.wait_ge(s_x, 48)
                        layer_norm(dve, link, xs, stats, mv, lambda: dve.wait_ge(s_rstd, 1), s_lnv, rstd)
                        dve.wait_ge(s_d, 1)
                        link(nc.vector.tensor_scalar(hn[:], hn[:], 0.0, None, ALU.max))
                        nc.vector.tensor_tensor(hn[:], hn[:], dis[:].unsqueeze(2).to_broadcast((P, NT, F)), ALU.mult).then_inc(s_h, 1)
                        dve.wait_ge(s_id, 1)
                        with dve.Fori(0, NT // 2) as k:
                            for s in range(2):
                                t = 2 * k + s
                                dve.wait_ge(s_lb[s], 16 * k + 16)
                                d = row[s][:, ds(t * P, P)]
                                nc.vector.tensor_tensor(d, d, ident[:], ALU.add).then_inc(s_eye, 1)
                                for e in range(ODD):
                                    g0, n = GROUPS[2 * e + 1]
                                    dve.wait_ge(s_tr1, ODD * t + e + 1)
                                    dve.wait_ge(s_ag, len(GROUPS) * t + 2 * e + 2)
                                    nc.vector.tensor_copy(aT[:, g0:g0 + n, :], tr[1][:, 0:n * P].rearrange("p (a b) -> p a b", b=P)).then_inc(s_ev1, 1)
                                dve.wait_ge(s_u, t + 1)
                                nc.vector.tensor_copy(o2[:, ds(t, 1), :], upd[:, 0:F].unsqueeze(1)).then_inc(s_uc, 1)
                        dve.wait_ge(s_uc, NT + 1)
                        link(nc.vector.tensor_tensor(o2[:], o2[:], dis[:].unsqueeze(2).to_broadcast((P, NT, F)), ALU.mult))
                        link(nc.vector.tensor_scalar(o2[:], o2[:], 0.0, None, ALU.max))
                        link(nc.vector.tensor_tensor(xs[:], xs[:], o2[:], ALU.add))

                    @block.tensor
                    def _(pe):
                        pe.sem_inc(s_ag, 7)
                        pe.wait_ge(s_h, 1)
                        pe.wait_ge(s_x, 48)
                        with pe.Fori(0, NT // 2) as k:
                            for s in range(2):
                                t = 2 * k + s
                                pe.wait_ge(s_lb[s], 16 * k + 16)
                                pe.wait_ge(s_eye, t + 1)

                                def products(g):
                                    g0, n = GROUPS[g]
                                    if g % 2 == 0:
                                        pe.wait_ge(s_ev0, EVEN * t + g // 2 + 2)
                                    else:
                                        pe.wait_ge(s_ev1, ODD * t + g // 2 + 2)
                                    if g == 0:
                                        pe.wait_ge(s_agc, t + 1)
                                    for m in range(g0, g0 + n):
                                        last = nc.tensor.matmul(agg[:, 0:P], hn[:, m, :], aT[:, m, :], start=(m == 0), stop=(m == NT - 1))
                                    last.then_inc(s_ag, 1)

                                for g, (g0, n) in enumerate(GROUPS):
                                    if g % 2 == 0:
                                        pe.wait_ge(s_ev0, EVEN * t + g // 2 + 1)
                                    else:
                                        pe.wait_ge(s_ev1, ODD * t + g // 2 + 1)
                                    for i in range(n):
                                        last = nc.tensor.transpose(tr[g % 2][:, i * P:(i + 1) * P], row[s][:, (g0 + i) * P:(g0 + i + 1) * P], ident[:])
                                    last.then_inc((s_tr0, s_tr1)[g % 2], 1)
                                    if g:
                                        products(g - 1)
                                products(len(GROUPS) - 1)
                                pe.wait_ge(s_agc, t + 2)
                                pe.wait_ge(s_uc, t + 1)
                                nc.tensor.matmul(upd[:, 0:F], aggs[:], w0s[:], start=True, stop=True).then_inc(s_u, 1)

            with ExitStack() as c2:
                sb, pb, sem = open_(c2)
                wst = sb("wst", [P, 3, H, F], fp32)
                wT = sb("wT", [F, 3, H * P], fp32)
                stats = sb("stats2", [P, NT, 6], fp32)
                mv = sb("mv2", [P, NT, 2], fp32)
                rstd = sb("rstd2", [P, NT], fp32)
                expo = sb("expo2", [P, NT], fp32)
                minus = sb("minus", [P, 3], bf16)
                hrow = sb("hrow", [P, F], fp32)
                hT = sb("hT", [F, P], fp32)
                full = [sb(f"full{i}", [P, H * P], fp32) for i in range(2)]
                parts = [sb("q_parts", [P, 6, H * P], bf16), sb("k_parts", [P, 3, H * P], bf16)]
                v_out = sb("v_out", [P, H * P], fp32)
                pj = [pb(f"pj{i}", [P, 2, 512], fp32) for i in range(3)]
                hTp = pb("hTp", [P, 512], fp32)
                s_w = sem("s_w")
                s_pad = sem("s_pad2")
                s_lnv = sem("s_lnv2")
                s_rstd = sem("s_rstd2")
                s_c = sem("s_c2")
                s_wt = sem("s_wt")
                s_wc = sem("s_wc")
                s_h = sem("s_h2")
                s_x1 = sem("s_x1")
                s_hr = sem("s_hr")
                s_ht = sem("s_ht")
                s_htc = sem("s_htc")
                s_pj = [sem(f"s_pj{i}") for i in range(3)]
                s_cp = [sem(f"s_cp{i}") for i in range(3)]
                s_sp = [sem(f"s_sp{i}") for i in range(2)]
                s_ng = sem("s_ng")
                s_o = [sem(f"s_o{i}") for i in range(3)]
                with nc.Block() as block:
                    @block.sync
                    def _(sp):
                        for i, w in enumerate((wq, wk, wv)):
                            sp.dma_start(wst[:, i, :, :], w.rearrange("(b h) f -> b h f", h=H)).then_inc(s_w, 16)
                        sp.dma_start(x1_rows, xs[:]).then_inc(s_x1, 16)
                        with sp.Fori(0, NT) as t:
                            for i, (rows, n) in enumerate(((q_rows, 6), (k_rows, 3))):
                                wait(sp, s_sp[i], t + 2)
                                if i == 0:
                                    wait(sp, s_ng, t + 1)
                                sp.dma_start(rows[ds(t * P, P), :, :], parts[i][:].rearrange("p s (h b) -> p (s h) b", b=P)).then_inc(s_o[i], 16)
                            wait(sp, s_cp[2], t + 2)
                            sp.dma_start(v_rows[ds(t * P, P), :, :], v_out[:].rearrange("p (h b) -> p h b", b=P)).then_inc(s_o[2], 16)
                        wait(sp, s_x1, 16)
                        for i in range(3):
                            wait(sp, s_o[i], 16 * NT + 16)

                    @block.gpsimd
                    def _(pool):
                        pool.memset(expo[:], -0.5).then_inc(s_pad, 1)
                        pool.memset(minus[:], -1.0).then_inc(s_pad, 1)
                        wait(pool, s_pad, 2)
                        wait(pool, s_lnv, 1)
                        nc.gpsimd.tensor_tensor(rstd[:], rstd[:], expo[:], ALU.pow).then_inc(s_rstd, 1)
                        with pool.Fori(0, NT) as t:
                            wait(pool, s_sp[0], t + 2)
                            wait(pool, s_o[0], 16 * t + 16)
                            nc.gpsimd.tensor_tensor(parts[0][:, 3:6, :], parts[0][:, 0:3, :], minus[:].unsqueeze(2).to_broadcast((P, 3, H * P)), ALU.mult).then_inc(s_ng, 1)

                    @block.scalar
                    def _(act):
                        act.sem_inc(s_o[0], 16)
                        act.sem_inc(s_o[1], 16)
                        act.sem_inc(s_o[2], 16)
                        for i in range(3):
                            act.sem_inc(s_cp[i], 1)
                            act.wait_ge(s_wt, i + 1)
                            nc.scalar.activation(wT[:, i, :].rearrange("p (a b) -> p a b", a=2), pj[i][:], ACT.Copy).then_inc(s_wc, 1)
                        act.wait_ge(s_h, 1)
                        with act.Fori(0, NT) as t:
                            act.wait_ge(s_ht, t + 1)
                            nc.scalar.activation(hrow[:], hn[:, ds(t, 1), :].rearrange("p a f -> p (a f)"), ACT.Copy).then_inc(s_hr, 1)
                            for i, c in ((0, HALF_SCALE), (1, 1.0)):
                                act.wait_ge(s_pj[i], t + 1)
                                act.wait_ge(s_sp[i], t + 1)
                                act.wait_ge(s_o[i], 16 * t + 16)
                                if i == 0:
                                    act.wait_ge(s_ht, t + 2)
                                nc.scalar.activation(full[i][:].rearrange("p (a b) -> p a b", a=2), pj[i][:], ACT.Copy, scale=c)
                                nc.scalar.activation(parts[i][:, 0, :].rearrange("p (a b) -> p a b", a=2), pj[i][:], ACT.Copy, scale=c).then_inc(s_cp[i], 1)
                            act.wait_ge(s_pj[2], t + 2)
                            act.wait_ge(s_o[2], 16 * t + 16)
                            nc.scalar.activation(v_out[:].rearrange("p (a b) -> p a b", a=2), pj[2][:], ACT.Copy).then_inc(s_cp[2], 1)

                    @block.vector
                    def _(dve):
                        chain = [0]

                        def link(ins):
                            chain[0] += 1
                            ins.then_inc(s_c, 1)
                            dve.wait_ge(s_c, chain[0])

                        dve.sem_inc(s_sp[0], 1)
                        dve.sem_inc(s_sp[1], 1)
                        layer_norm(dve, link, xs, stats, mv, lambda: dve.wait_ge(s_rstd, 1), s_lnv, rstd)
                        nc.vector.tensor_scalar(hn[:], hn[:], 0.0, None, ALU.max).then_inc(s_h, 1)
                        base = chain[0]
                        with dve.Fori(0, NT) as t:
                            dve.wait_ge(s_ht, t + 2)
                            dve.wait_ge(s_pj[2], t + 1)
                            nc.vector.tensor_copy(hT[:], hTp[:, 0:P]).then_inc(s_htc, 1)
                            for i in range(2):
                                dve.wait_ge(s_cp[i], t + 2)
                                a = full[i]
                                nc.vector.tensor_tensor(a[:], a[:], parts[i][:, 0, :], ALU.subtract).then_inc(s_c, 1)
                                dve.wait_ge(s_c, base + 4 * t + 2 * i + 1)
                                nc.vector.tensor_copy(parts[i][:, 1, :], a[:]).then_inc(s_c, 1)
                                dve.wait_ge(s_c, base + 4 * t + 2 * i + 2)
                                nc.vector.tensor_tensor(parts[i][:, 2, :], a[:], parts[i][:, 1, :], ALU.subtract).then_inc(s_sp[i], 1)

                    @block.tensor
                    def _(pe):
                        pe.sem_inc(s_ht, 1)
                        pe.sem_inc(s_pj[2], 1)
                        for i in range(3):
                            pe.wait_ge(s_w, 48)
                            for h in range(H):
                                last = nc.tensor.transpose(pj[i][:, h // 4, (h % 4) * P:(h % 4 + 1) * P], wst[:, i, h, :], ident[:])
                            last.then_inc(s_wt, 1)
                        pe.wait_ge(s_wc, 3)
                        with pe.Fori(0, NT) as t:
                            pe.wait_ge(s_hr, t + 1)
                            nc.tensor.transpose(hTp[:, 0:P], hrow[:], ident[:]).then_inc(s_ht, 1)
                            pe.wait_ge(s_htc, t + 1)
                            for i in range(3):
                                pe.wait_ge(s_cp[i], t + 1)
                                for a in range(2):
                                    last = nc.tensor.matmul(pj[i][:, a, :], hT[:], wT[:, i, a * 512:(a + 1) * 512], start=True, stop=True)
                                last.then_inc(s_pj[i], 1)

            with ExitStack() as c3:
                sb, pb, sem = open_(c3)
                vin = [sb(f"vin{i}", [P, NP], fp32) for i in range(2)]
                vout = [sb(f"vout{i}", [P, NT, P], fp32) for i in range(2)]
                tr = [pb(f"vtr{i}", [P, 512], fp32) for i in range(2)]
                s_vl = [sem(f"s_vl{i}") for i in range(2)]
                s_tr = [sem(f"s_vtr{i}") for i in range(2)]
                s_ev = [sem(f"s_vev{i}") for i in range(2)]
                s_vs = [sem(f"s_vs{i}") for i in range(2)]
                GROUPS = [(4 * i, min(4, NT - 4 * i)) for i in range((NT + 3) // 4)]
                CNT = ((len(GROUPS) + 1) // 2, len(GROUPS) // 2)
                vt_g = vt.rearrange("(g t p) c -> p g t c", g=NG, p=P)
                v_gh = v_heads.rearrange("h d m -> d h m")

                def copier(eng, b, copy):
                    with eng.Fori(0, NG // 2) as k:
                        for s in range(2):
                            eng.wait_ge(s_vs[s], 16 * k + 16)
                            for e in range(CNT[b]):
                                g0, n = GROUPS[2 * e + b]
                                eng.wait_ge(s_tr[b], CNT[b] * (2 * k + s + 2) + e + 1)
                                copy(vout[s][:, g0:g0 + n, :], tr[b][:, 0:n * P].rearrange("p (a b) -> p a b", b=P)).then_inc(s_ev[b], 1)

                with nc.Block() as block:
                    @block.gpsimd
                    def _(pool):
                        with pool.Fori(0, NG // 2) as k:
                            for s in range(2):
                                for b in range(2):
                                    wait(pool, s_tr[b], CNT[b] * (2 * k + s + 1))
                                for d in range(GH):
                                    pool.dma_start(vin[s][d * H:(d + 1) * H, :], v_heads[:, ds((2 * k + s) * GH + d, 1), :].rearrange("h a m -> (h a) m")).then_inc(s_vl[s], 16)

                    @block.sync
                    def _(sp):
                        with sp.Fori(0, NG // 2) as k:
                            for s in range(2):
                                wait(sp, s_ev[0], CNT[0] * (2 * k + s + 1) + 1)
                                wait(sp, s_ev[1], CNT[1] * (2 * k + s + 1) + 1)
                                sp.dma_start(vt_g[:, ds(2 * k + s, 1), :, :].rearrange("p g t c -> p (g t) c"), vout[s][:]).then_inc(s_vs[s], 16)
                        for s in range(2):
                            wait(sp, s_vs[s], 16 * (NG // 2) + 16)

                    @block.scalar
                    def _(act):
                        act.sem_inc(s_ev[0], 1)
                        act.sem_inc(s_vs[0], 16)
                        act.sem_inc(s_vs[1], 16)
                        copier(act, 0, lambda o, i: nc.scalar.activation(o, i, ACT.Copy))

                    @block.vector
                    def _(dve):
                        dve.sem_inc(s_ev[1], 1)
                        copier(dve, 1, nc.vector.tensor_copy)

                    @block.tensor
                    def _(pe):
                        for b in range(2):
                            pe.sem_inc(s_tr[b], 2 * CNT[b])
                        with pe.Fori(0, NG // 2) as k:
                            for s in range(2):
                                pe.wait_ge(s_vl[s], 16 * GH * (k + 1))
                                for g, (g0, n) in enumerate(GROUPS):
                                    pe.wait_ge(s_ev[g % 2], CNT[g % 2] * (2 * k + s) + g // 2 + 1)
                                    for i in range(n):
                                        last = nc.tensor.transpose(tr[g % 2][:, i * P:(i + 1) * P], vin[s][:, (g0 + i) * P:(g0 + i + 1) * P], ident[:])
                                    last.then_inc(s_tr[g % 2], 1)

        with ExitStack() as c4:
            sb, pb, sem = open_(c4)
            k_res = sb("k_res", [P, GH, NP], bf16)
            q_blk = [sb(f"q_blk{i}", [P, GH, CB], bf16) for i in range(2)]
            mk = sb("mk", [P, GH // 2, CH], bf16)
            mq = [sb(f"mq{i}", [P, GH, P], bf16) for i in range(2)]
            adj_row = sb("adj_row", [P, 2, CH], fp32)
            adj_blk = sb("adj_blk", [CS, 4, 2 * P], fp32)
            v_in = [sb(f"v_in{i}", [P, 2, GH * H], fp32) for i in range(2)]
            v_pad = sb("v_pad", [P, 2, GH, 32], fp32)
            prob = sb("prob", [P, 2, SLOTS, CB], fp32)
            o_sb = sb("o_sb", [P, 2, CB], fp32)
            rec = sb("rec", [P, CB], fp32)
            m_part = [sb(f"m_part{i}", [P, GH], fp32) for i in range(2)]
            m_run = sb("m_run", [P, GH, NT], fp32)
            m_split = sb("m_split", [P, 3, GH * NT], bf16)
            m_rows = adj_row[:].rearrange("p a b -> p (a b)").bitcast(bf16)[:, 0:4 * 6 * P].rearrange("p (a s b) -> p a s b", a=4, s=6)
            ident_f = sb("ident_f", [CS, CS], fp32)
            ident_b = sb("ident_b", [P, P], bf16)
            spread = sb("spread", [P, P], fp32)
            O = [pb(f"O{i}", [P, 512], fp32) for i in range(2)]
            S = pb("S", [P, 2, 512], fp32)
            X = [pb(f"X{i}", [P, 2, 512], fp32) for i in range(2)]
            s_set = sem("s_set")
            s_dset = sem("s_dset")
            s_kr = sem("s_kr")
            s_q = [sem(f"s_q{i}") for i in range(2)]
            s_ab = sem("s_ab")
            s_tr = sem("s_tr")
            s_vl = [sem(f"s_vi{i}") for i in range(2)]
            s_vp = sem("s_vp")
            s_sa, s_sb = sem("s_sa"), sem("s_sb")
            s_ea, s_eb = sem("s_ea"), sem("s_eb")
            s_pa, s_pb = sem("s_pa"), sem("s_pb")
            s_oc = sem("s_oc")
            s_bc = sem("s_bc")
            s_rc = sem("s_rc")
            s_fc = sem("s_fc")
            s_on = sem("s_on")
            s_od = sem("s_od")
            s_mk = sem("s_mk")
            s_mq = [sem(f"s_mq{i}") for i in range(2)]
            s_ad = [sem(f"s_ad{i}") for i in range(2)]
            s_x = sem("s_x")
            s_tt = sem("s_tt")
            s_mu = sem("s_mu")
            s_mi = sem("s_mi")
            s_ms = sem("s_ms")
            s_mt = sem("s_mt")
            s_me = sem("s_me")
            s_mw = sem("s_mw")
            PAIRS = (NPAIR - 1) // 2
            SB0, VP0, X0, TT0 = 209, 5, 33, 18

            adjp_blk = adjp.rearrange("(b s p) m -> p (b s) m", s=4, p=CS)
            q_pairs, k_pairs = (v.rearrange("r (a b) m -> r a b m", b=2) for v in (q_heads, k_heads))
            vt_v = vt.rearrange("(t p) c -> p t c", p=P)
            mx_rows = mx.rearrange("s h (t p) -> (h t) s p", p=P)
            ost_v = ost.rearrange("(g p) m -> p g m", p=P)

            def slot(d):
                return d % SLOTS

            def place(d):
                return (d // 4) % 2, 32 * (d % 4), 16 * (d // 8)

            def sweep(eng, g, body, finish=None, peel=False):
                def chunk(o):
                    c = g * NCH + o
                    n0, u0 = c * BODIES, c * (BODIES // 2)
                    body(n0, 2 * o, 0, 0, o, 0, u0, True)
                    with eng.Fori(0, PAIRS) as p:
                        body(n0 + 2 * p + 1, 2 * o, 2 * p + 1, 2 * p + 1, o, 1, u0 + p, False)
                        body(n0 + 2 * p + 2, 2 * o, 2 * p + 2, 2 * p + 2, o, 0, u0 + p + 1, False)
                    if finish:
                        finish(c * 2, 2 * o)
                    body(n0 + NPAIR, 2 * o + 1, 0, NPAIR, o, 1, u0 + PAIRS, True)
                    with eng.Fori(0, PAIRS) as p:
                        body(n0 + 2 * p + NPAIR + 1, 2 * o + 1, 2 * p + 1, 2 * p + NPAIR + 1, o, 0, u0 + p + PAIRS + 1, False)
                        body(n0 + 2 * p + NPAIR + 2, 2 * o + 1, 2 * p + 2, 2 * p + NPAIR + 2, o, 1, u0 + p + PAIRS + 1, False)
                    if finish:
                        finish(c * 2 + 1, 2 * o + 1)

                with eng.Fori(0, NCH - 1 if peel else NCH) as o:
                    chunk(o)
                if peel:
                    chunk(NCH - 1)

            def schedule(eng, run, maxima_end):
                run(None, 0)
                maxima_end(0)
                with eng.Fori(0, NG - 1) as g:
                    run(g, 1)
                    maxima_end(g + 1)
                run(NG - 1, None)

            AHEAD = BODIES * NCH

            with nc.Block() as block:
                @block.sync
                def _(sp):
                    sp.sem_inc(s_od, 16)
                    sp.sem_inc(s_kr, 16)
                    wait(sp, s_set, 2)
                    wait(sp, s_dset, 5)

                    def load_keys(g, pair, done):
                        if done is not None:
                            wait(sp, s_sb, done * GH + SB0)
                        wait(sp, s_kr, (g * NPAIR + pair) * 192 + 16)
                        h0, keys = g * GH, ds(pair * (2 * P), 2 * P)
                        for r, p in enumerate((0, 0, 0, 1, 1, 2)):
                            sp.dma_start(k_res[8 * r:8 * r + 8, :, keys], k_heads[8 * p:8 * p + 8, ds(h0, GH), keys]).then_inc(s_kr, 16)
                            sp.dma_start(k_res[KR + 8 * r:KR + 8 * r + 8, 1:GH, keys], k_heads[8 * p:8 * p + 8, ds(h0, GH - 1), keys]).then_inc(s_kr, 16)

                    def load_queries(g, idx, blk, h):
                        wait(sp, s_sb, idx * (NPAIR * GH) + 1)
                        h0, cols = g * GH, ds(blk * CB, CB)
                        for r, n in ((0, 3), (3, 2), (5, 1)):
                            sp.dma_start(q_blk[h][8 * r:8 * (r + n), :, :], q_heads[0:8 * n, ds(h0, GH), cols]).then_inc(s_q[h], 16)
                            sp.dma_start(q_blk[h][KR + 8 * r:KR + 8 * (r + n), 1:GH, :], q_heads[24:24 + 8 * n, ds(h0, GH - 1), cols]).then_inc(s_q[h], 16)
                        sp.dma_start(q_blk[h][96:99, :, :], mx[0:3, ds(h0, GH), cols]).then_inc(s_q[h], 16)
                        sp.dma_start(q_blk[h][99:102, 1:GH, :], mx[3:6, ds(h0, GH - 1), cols]).then_inc(s_q[h], 16)

                    def run(gm, gx):
                        both = gm is not None and gx is not None
                        g = gm if gm is not None else gx
                        def body(n, blk, pair, t, o, par, u, first):
                            if gm is not None and first:
                                load_queries(gm, (gm * NCH + o) * 2 + par, blk, par)
                            if gx is not None:
                                nx = n + AHEAD if both else n
                                gg = gm + 1 if both else gx
                                wait(sp, s_tt, nx * GH + 2)
                                sp.dma_start(adj_row[:, par, :], adjp[ds(t * P, P), ds(o * CH, CH)]).then_inc(s_ad[par], 16)
                                wait(sp, s_x, nx * GH + 17)
                                for odd in range(2):
                                    for r, m in ((0, 1), (1, 2)):
                                        sp.dma_start(mq[par][64 * odd + 8 * r:64 * odd + 8 * (r + m), odd::2, :],
                                                     q_pairs[0:8 * m, ds(gg * (GH // 2), GH // 2), odd, ds(t * P, P)]).then_inc(s_mq[par], 16)
                                if first and par == 0:
                                    wait(sp, s_x, nx * GH + X0)
                                    for odd in range(2):
                                        for r, m in ((0, 2), (2, 1)):
                                            sp.dma_start(mk[64 * odd + 8 * r:64 * odd + 8 * (r + m), :, :],
                                                         k_pairs[0:8 * m, ds(gg * (GH // 2), GH // 2), odd, ds(o * CH, CH)]).then_inc(s_mk, 16)
                            if gm is not None:
                                wait(sp, s_vp, n * 4 + 1)
                                sp.dma_start(v_in[par][:], vt_v[:, ds(gm * NT + 2 * pair, 2), :]).then_inc(s_vl[par], 16)
                                wait(sp, s_tr, n + 1)
                                sp.dma_start(adj_blk[:], adjp_blk[:, ds(blk * 4, 4), ds(pair * (2 * P), 2 * P)]).then_inc(s_ab, 16)
                            if both and isinstance(o, int) and blk == NB - 1 and not first:
                                load_keys(gm + 1, pair - 1, n)

                        def finish(idx, blk):
                            wait(sp, s_on, idx + 1)
                            sp.dma_start(ost_v[:, ds(gm * 2, 2), ds(blk * CB, CB)], o_sb[:]).then_inc(s_od, 16)

                        sweep(sp, g, body, finish if gm is not None else None, peel=both)
                        if both:
                            load_keys(gm + 1, NPAIR - 1, (gm + 1) * AHEAD)
                        if gm is None:
                            with sp.Fori(0, NPAIR) as pair:
                                load_keys(0, pair, None)

                    def maxima_end(g):
                        wait(sp, s_me, g + 1)
                        for a in range(4):
                            w = min(P, GH * NT - a * P)
                            sp.dma_start(mx_rows[ds(g * (GH * NT) + a * P, w), :, :], m_rows[0:w, a, :, :]).then_inc(s_mw, 16)
                        wait(sp, s_mw, g * 64 + 64)

                    schedule(sp, run, maxima_end)
                    wait(sp, s_od, 16 * NG * NB + 16)

                @block.gpsimd
                def _(pool):
                    pool.sem_inc(s_vp, VP0)
                    identity(pool, ident_b[:], P, s_set, s_set)
                    wait(pool, s_set, 2)
                    pool.memset(spread[:], 0.0).then_inc(s_set, 1)
                    wait(pool, s_set, 3)
                    pool.affine_select(out=spread[:].rearrange("p (a b) -> p a b", b=16), in_=spread[:].rearrange("p (a b) -> p a b", b=16),
                                       compare_op=ALU.not_equal, fill=1.0, base=-8, pattern=[[-16, 8], [0, 16]],
                                       channel_multiplier=1).then_inc(s_set, 1)
                    wait(pool, s_set, 4)
                    pool.memset(ident_f[:], 0.0).then_inc(s_set, 1)
                    wait(pool, s_set, 5)
                    pool.affine_select(out=ident_f[:], in_=ident_f[:], compare_op=ALU.not_equal, fill=1.0, base=0,
                                       pattern=[[-1, CS]], channel_multiplier=1).then_inc(s_set, 1)
                    wait(pool, s_dset, 6)

                    def run(gm, gx):
                        if gm is None:
                            return

                        def body(n, blk, pair, t, o, par, u, first):
                            wait(pool, s_vl[par], u * 16 + 16)
                            for q in range(4):
                                wait(pool, s_pb, n * 4 + q + 1)
                                c = 16 * (q // 2)
                                nc.gpsimd.tensor_copy(v_pad[:, :, 4 * q:4 * q + 4, c:c + H],
                                                      v_in[par][:, :, 4 * q * H:4 * (q + 1) * H].rearrange("p t (d h) -> p t d h", h=H)).then_inc(s_vp, 1)
                        sweep(pool, gm, body)

                    schedule(pool, run, lambda g: None)

                @block.scalar
                def _(act):
                    act.sem_inc(s_ea, 1)
                    act.sem_inc(s_eb, 1)

                    def run(gm, gx):
                        if gm is None:
                            return

                        def body(n, blk, pair, t, o, par, u, first):
                            for d in range(GH):
                                for i, (sc, pv, ex) in enumerate(((s_sa, s_pa, s_ea), (s_sb, s_pb, s_eb))):
                                    act.wait_ge(pv, n * 4 + d // 4 + 3)
                                    act.wait_ge(sc, n * GH + d + 1 + (SB0 if i else 0))
                                    nc.scalar.activation(prob[:, i, slot(d), :], S[:, i, 0:CB], ACT.Exp, scale=2.0).then_inc(ex, 1)

                        def finish(idx, blk):
                            act.wait_ge(s_pb, idx * (4 * NPAIR) + 4 * NPAIR + 4)
                            act.wait_ge(s_od, idx * 16 + 16)
                            for b in range(2):
                                last = nc.scalar.activation(o_sb[:, b, :], O[b][:, 0:CB], ACT.Copy)
                            last.then_inc(s_oc, 1)
                        sweep(act, gm, body, finish)

                    schedule(act, run, lambda g: None)

                @block.vector
                def _(dve):
                    for b in range(2):
                        nc.vector.memset(mq[b][0:XR, :, :], 0.0).then_inc(s_dset, 1)
                    nc.vector.memset(mk[0:XR, :, :], 0.0).then_inc(s_dset, 1)
                    for b in range(2):
                        nc.vector.memset(q_blk[b][:, 0, :], 0.0)
                    nc.vector.memset(k_res[0:96, 0, :], 0.0).then_inc(s_dset, 1)
                    nc.vector.memset(k_res[96:102, :, :], 1.0).then_inc(s_dset, 1)
                    nc.vector.memset(v_pad[:], 0.0).then_inc(s_fc, 1)
                    dve.wait_ge(s_fc, 1)
                    nc.vector.memset(v_pad[:, :, 0:GH // 2, 8:9], 1.0)
                    nc.vector.memset(v_pad[:, :, GH // 2:GH, 24:25], 1.0).then_inc(s_dset, 1)
                    dve.sem_inc(s_rc, 1)
                    dve.sem_inc(s_tt, TT0)
                    dve.sem_inc(s_mu, 2)

                    def run(gm, gx):
                        both = gm is not None and gx is not None
                        g = gm if gm is not None else gx
                        if gx is not None:
                            nc.vector.memset(m_run[:], LOW).then_inc(s_mi, 1)

                        def body(n, blk, pair, t, o, par, u, first):
                            if gx is None:
                                return
                            nx = n + AHEAD if both else n
                            ux = u + AHEAD // 2 if both else u
                            dve.wait_ge(s_ad[par], ux * 16 + 16)
                            dve.wait_ge(s_mu, nx + 1)
                            for k in range(GH):
                                wait(dve, s_x, nx * GH + k + 1 + X0)
                                x_ = X[k % 2][:, :, 0:CB]
                                nc.vector.tensor_tensor_reduce(out=x_, in0=x_, in1=adj_row[:, par, :].rearrange("p (a b) -> p a b", a=2),
                                                               scale=1.0, scalar=LOW, op0=ALU.add, op1=ALU.max,
                                                               accum_out=m_part[par][:, k:k + 1]).then_inc(s_tt, 1)
                            if first and par == 0:
                                dve.wait_ge(s_mi, (gm + 2) if both else gx + 1)
                            dve.wait_ge(s_tt, nx * GH + GH + TT0)
                            m = m_run[:, :, ds(t, 1)]
                            nc.vector.tensor_tensor(m, m, m_part[par][:].unsqueeze(2), ALU.max).then_inc(s_mu, 1)

                        def finish(idx, blk):
                            for b in range(2):
                                dve.wait_ge(s_bc, idx + 1)
                                dve.wait_ge(s_fc, idx * 4 + 2 * b + 1)
                                nc.vector.reciprocal(rec[:], O[b][:, 0:CB]).then_inc(s_fc, 1)
                                dve.wait_ge(s_fc, idx * 4 + 2 * b + 2)
                                if b == 1:
                                    dve.sem_inc(s_rc, 1)
                                last = nc.vector.tensor_tensor(o_sb[:, b, :], o_sb[:, b, :], rec[:], ALU.mult)
                                last.then_inc(s_fc, 1)
                            dve.wait_ge(s_fc, idx * 4 + 5)
                            dve.sem_inc(s_on, 1)
                        sweep(dve, g, body, finish if gm is not None else None)

                    def maxima_end(g):
                        m = m_run[:].rearrange("p h t -> p (h t)")
                        dve.wait_ge(s_mu, g * AHEAD + AHEAD + 2)
                        base = g * 5
                        nc.vector.tensor_scalar(m_split[:, 0, :], m, -1.0, None, ALU.mult).then_inc(s_ms, 1)
                        dve.wait_ge(s_ms, base + 1)
                        nc.vector.scalar_tensor_tensor(m, m, -1.0, m_split[:, 0, :], ALU.mult, ALU.subtract).then_inc(s_ms, 1)
                        dve.wait_ge(s_ms, base + 2)
                        nc.vector.tensor_copy(m_split[:, 1, :], m).then_inc(s_ms, 1)
                        dve.wait_ge(s_ms, base + 3)
                        nc.vector.tensor_tensor(m, m, m_split[:, 1, :], ALU.subtract).then_inc(s_ms, 1)
                        dve.wait_ge(s_ms, base + 4)
                        nc.vector.tensor_copy(m_split[:, 2, :], m).then_inc(s_ms, 1)
                        dve.wait_ge(s_ms, base + 5)
                        dve.wait_ge(s_mt, g + 1)
                        for a in range(4):
                            w = min(P, GH * NT - a * P)
                            b = X[a // 2][0:w, a % 2, :].bitcast(bf16)[:, 0:3 * P].rearrange("p (s b) -> p s b", s=3)
                            nc.vector.tensor_copy(m_rows[0:w, a, 0:3, :], b)
                            last = nc.vector.tensor_scalar(m_rows[0:w, a, 3:6, :], b, -1.0, None, ALU.mult)
                        last.then_inc(s_me, 1)
                        dve.wait_ge(s_me, g + 1)

                    schedule(dve, run, maxima_end)

                @block.tensor
                def _(pe):
                    pe.sem_inc(s_tr, 1)
                    pe.sem_inc(s_sb, SB0)
                    pe.sem_inc(s_pa, 4)
                    pe.sem_inc(s_pb, 4)
                    pe.sem_inc(s_x, X0)
                    pe.wait_ge(s_set, 6)
                    pe.wait_ge(s_dset, 6)

                    def run(gm, gx):
                        both = gm is not None and gx is not None
                        g = gm if gm is not None else gx
                        def values(n, b, i, half, first):
                            if half == 0:
                                pe.wait_ge(s_vp, n * 4 + b + 1 + VP0)
                                pe.wait_ge((s_ea, s_eb)[i], n * GH + 4 * b + 4 + 1)
                            cols = slice(half * (CB // 2), (half + 1) * (CB // 2))
                            for d in range(4 * b, 4 * b + 4):
                                bank, r, c = place(d)
                                last = nc.tensor.matmul(O[bank][r:r + 32, cols], v_pad[:, i, d, :], prob[:, i, slot(d), cols],
                                                        start=(first and i == 0 and c == 0 and half == 0), stop=True, skip_group_check=True)
                            if half == 1:
                                last.then_inc((s_pa, s_pb)[i], 1)

                        def body(n, blk, pair, t, o, par, u, first):
                            nx = n + AHEAD if both else n
                            ux = u + AHEAD // 2 if both else u

                            def maximum(k):
                                pe.wait_ge(s_tt, nx * GH + k + 17)
                                for a in range(2):
                                    last = nc.tensor.matmul(X[k % 2][:, a, 0:CB], mq[par][0:XR, k, :], mk[0:XR, k // 2, a * CB:(a + 1) * CB], start=True, stop=True)
                                last.then_inc(s_x, 1)

                            def bias(i):
                                pe.wait_ge((s_ea, s_eb)[i], n * GH + 1)
                                for c in range(4):
                                    last = nc.tensor.matmul(S[:, i, c * CS:(c + 1) * CS], adj_blk[:, c, i * P:(i + 1) * P], ident_f[:], start=(c == 0), stop=True,
                                                            is_transpose=True, skip_group_check=True)
                                if i == 1:
                                    last.then_inc(s_tr, 1)

                            def scores(d, i, q):
                                if d:
                                    pe.wait_ge((s_ea, s_eb)[i], n * GH + d + 1)
                                nc.tensor.matmul(S[:, i, 0:CB], k_res[0:102, d, ds((2 * pair + i) * P, P)], q[0:102, d, :],
                                                 start=False, stop=True, skip_group_check=True).then_inc((s_sa, s_sb)[i], 1)

                            if gx is not None:
                                pe.wait_ge(s_mq[par], ux * 64 + 64)
                                if first and par == 0:
                                    pe.wait_ge(s_mk, (((gm + 1) if both else gx) * NCH + o) * 64 + 64)
                            if gm is not None:
                                q = q_blk[body.block_parity]
                                if first:
                                    pe.wait_ge(s_q[par], (gm * NCH + o) * 128 + 128)
                                wait(pe, s_kr, (gm * NPAIR + pair) * 192 + 192 + 16)
                                pe.wait_ge(s_ab, n * 16 + 16)
                            for d in range(GH):
                                if gm is not None:
                                    if d == 0:
                                        bias(0)
                                    scores(d, 0, q)
                                if gx is not None:
                                    maximum(d)
                                if gm is not None:
                                    if d == 0:
                                        bias(1)
                                    scores(d, 1, q)
                                    if d == 4 and first:
                                        pe.wait_ge(s_rc, (gm * NCH + o) * 2 + par + 1)
                                    if d >= 4:
                                        values(n, d // 4 - 1, d % 4 // 2, d % 2, first)
                                    elif not first:
                                        values(n - 1, 3, d // 2, d % 2, False)

                        body.block_parity = 0

                        def counted(n, blk, pair, t, o, par, u, first):
                            if first:
                                body.block_parity = par
                            body(n, blk, pair, t, o, par, u, first)

                        def finish(idx, blk):
                            for i in range(4):
                                values(idx * NPAIR + NPAIR - 1, 3, i // 2, i % 2, False)
                            pe.wait_ge(s_oc, idx + 1)
                            for b in range(2):
                                last = nc.tensor.matmul(O[b][:, 0:CB], spread[:], o_sb[:, b, :], start=True, stop=True, skip_group_check=True)
                            last.then_inc(s_bc, 1)
                        sweep(pe, g, counted, finish if gm is not None else None)

                    def maxima_end(g):
                        pe.wait_ge(s_ms, g * 5 + 5)
                        for a in range(4):
                            w = min(P, GH * NT - a * P)
                            b = X[a // 2][0:w, a % 2, :].bitcast(bf16)
                            for s in range(3):
                                last = nc.tensor.transpose(b[:, s * P:(s + 1) * P], m_split[:, s, a * P:a * P + w], ident_b[:])
                        last.then_inc(s_mt, 1)

                    schedule(pe, run, maxima_end)

        with ExitStack() as c5:
            sb, pb, sem = open_(c5)
            zero = sb("zero", [H, P], fp32)
            ident = sb("ident3", [P, P], fp32)
            wo_s = sb("wo_s", [F, P, H], fp32)
            wo_T = sb("wo_T", [P, H, F], fp32)
            x1s = sb("x1s", [P, NT, F], fp32)
            res = sb("res", [P, NT, F], fp32)
            oh_in = [sb(f"oh_in{i}", [P, H, P], fp32) for i in range(2)]
            oh_T = [sb(f"oh_T{i}", [P, H, P], fp32) for i in range(2)]
            tr = [[pb(f"etr{i}{j}", [P, 512], fp32) for j in range(2)] for i in range(2)]
            pr = [pb(f"epr{i}", [P, 512], fp32) for i in range(2)]
            s_set = sem("s_eset")
            s_z = sem("s_ez")
            s_w = sem("s_ew")
            s_oh = sem("s_eoh")
            s_in = [sem(f"s_ein{i}") for i in range(2)]
            s_tr = [[sem(f"s_etr{i}{j}") for j in range(2)] for i in range(2)]
            s_tc = [[sem(f"s_etc{i}{j}") for j in range(2)] for i in range(2)]
            s_pr = [sem(f"s_epr{i}") for i in range(2)]
            s_ad = [sem(f"s_ead{i}") for i in range(2)]
            s_out = sem("s_eout")
            with nc.Block() as block:
                @block.sync
                def _(sp):
                    wait(sp, s_z, 1)
                    sp.dma_start(oh_t.ap()[:, N * P:GP], zero[:]).then_inc(s_oh, 16)
                    for g in range(NG):
                        for hf in range(2):
                            src = bass.AP(o_t, (g * 2 * P + 16 * hf) * NP, [[P * NP, 2], [32 * NP, 4], [NP, H], [1, N]])
                            dst = bass.AP(oh_t, (g * GH + 8 * hf) * N, [[4 * N, 2], [N, 4], [GP, H], [1, N]])
                            for b in range(2):
                                sp.dma_start(dst[b], src[b]).then_inc(s_oh, 16)
                    sp.dma_start(wo_s[:], wo.rearrange("f (b h) -> f b h", h=H)).then_inc(s_w, 16)
                    sp.dma_start(x1s[:], x1_rows).then_inc(s_w, 16)
                    wait(sp, s_oh, 16 * (4 * NG + 1))
                    with sp.Fori(0, NT // 2) as k:
                        for s in range(2):
                            for j in range(2):
                                wait(sp, s_tr[s][j], k + (2 if s == 0 else 1))
                            sp.dma_start(oh_in[s][:], oh_rows[ds((2 * k + s) * P, P), :, :]).then_inc(s_in[s], 16)
                    for s in range(2):
                        wait(sp, s_ad[s], NT // 2 + 1)
                    sp.dma_start(out[0:(NT - 1) * P, :].rearrange("(t p) f -> p t f", p=P), res[:, 0:NT - 1, :]).then_inc(s_out, 16)
                    sp.dma_start(out[(NT - 1) * P:N, :], res[0:LAST, NT - 1, :]).then_inc(s_out, 16)
                    wait(sp, s_out, 32)

                @block.gpsimd
                def _(pool):
                    identity(pool, ident[:], P, s_set, s_set)

                @block.scalar
                def _(act):
                    for h in range(0, H, 4):
                        act.wait_ge(s_tr[0][h // 4], 2)
                        nc.scalar.activation(wo_T[:, h:h + 4, :], tr[0][h // 4][:].rearrange("p (a b) -> p a b", a=4), ACT.Copy).then_inc(s_tc[0][0], 1)
                    with act.Fori(0, NT // 2) as k:
                        for s in range(2):
                            act.wait_ge(s_pr[s], k + 1)
                            act.wait_ge(s_tr[s][0], k + (3 if s == 0 else 2))
                            nc.scalar.activation(oh_T[s][:, 0:4, :], tr[s][0][:].rearrange("p (a b) -> p a b", a=4), ACT.Copy).then_inc(s_tc[s][0], 1)

                @block.vector
                def _(dve):
                    nc.vector.memset(zero[:], 0.0).then_inc(s_z, 1)
                    dve.sem_inc(s_ad[0], 1)
                    dve.sem_inc(s_ad[1], 1)
                    dve.wait_ge(s_w, 32)
                    with dve.Fori(0, NT // 2) as k:
                        for s in range(2):
                            dve.wait_ge(s_pr[s], k + 1)
                            dve.wait_ge(s_tr[s][1], k + (3 if s == 0 else 2))
                            nc.vector.tensor_copy(oh_T[s][:, 4:8, :], tr[s][1][:].rearrange("p (a b) -> p a b", a=4)).then_inc(s_tc[s][1], 1)
                            dve.wait_ge(s_pr[s], k + 2)
                            at = ds(2 * k + s, 1)
                            nc.vector.tensor_tensor(res[:, at, :], x1s[:, at, :], pr[s][:, 0:F].unsqueeze(1), ALU.add).then_inc(s_ad[s], 1)

                @block.tensor
                def _(pe):
                    for s in range(2):
                        pe.sem_inc(s_pr[s], 1)
                        for j in range(2):
                            pe.sem_inc(s_tr[s][j], 1)
                    pe.wait_ge(s_set, 2)
                    pe.wait_ge(s_w, 32)
                    for h in range(H):
                        last = nc.tensor.transpose(tr[0][h // 4][:, (h % 4) * P:(h % 4 + 1) * P], wo_s[:, :, h], ident[:])
                        if h % 4 == 3:
                            last.then_inc(s_tr[0][h // 4], 1)
                    pe.wait_ge(s_tc[0][0], 2)
                    with pe.Fori(0, NT // 2) as k:
                        for s in range(2):
                            pe.wait_ge(s_in[s], k * 16 + 16)
                            for h in range(H):
                                last = nc.tensor.transpose(tr[s][h // 4][:, (h % 4) * P:(h % 4 + 1) * P], oh_in[s][:, h, :], ident[:])
                                if h % 4 == 3:
                                    last.then_inc(s_tr[s][h // 4], 1)
                            pe.wait_ge(s_tc[s][0], k + (3 if s == 0 else 1))
                            pe.wait_ge(s_tc[s][1], k + 1)
                            pe.wait_ge(s_ad[s], k + 1)
                            for h in range(H):
                                last = nc.tensor.matmul(pr[s][:, 0:F], oh_T[s][:, h, :], wo_T[:, h, :], start=(h == 0), stop=(h == H - 1))
                            last.then_inc(s_pr[s], 1)

_INS = ['x', 'adj', 'L0_gnn_weight', 'L1_gnn_Wq', 'L1_gnn_Wk', 'L1_gnn_Wv', 'L1_gnn_Wo']


def kernel(**inputs):
    import numpy as _np
    import concourse.bacc as _bacc
    from concourse import mybir as _mybir
    from concourse.bass_utils import run_bass_kernel_spmd as _run

    nc = _bacc.Bacc("TRN2", target_bir_lowering=False, num_devices=1)
    arrays, args = {}, []
    for name in _INS:
        a = _np.ascontiguousarray(inputs[name])
        arrays[f"in_{name}"] = a
        args.append(nc.dram_tensor(f"in_{name}", a.shape, _mybir.dt.from_np(a.dtype), kind="ExternalInput").ap())
    n, f = inputs["x"].shape
    args.append(nc.dram_tensor("out_0", (n, f), _mybir.dt.float32, kind="ExternalOutput").ap())
    graph_layers_kernel(nc, *args)
    r = _run(nc, [arrays], core_ids=[0])
    return r.results[0]["out_0"]
```
